# Optimizing a Trainium2 kernel written in Bass

```python
import numpy as np
import jax
import jax.numpy as jnp

def _softmax(x, axis=-1):
    return jax.nn.softmax(x, axis=axis)
def _gelu(x):
    return jax.nn.gelu(x, approximate=True)
def _silu(x):
    return jax.nn.silu(x)
def _sigmoid(x):
    return jax.nn.sigmoid(x)
def _layernorm(x, axis=-1, eps=1e-5):
    m = jnp.mean(x, axis=axis, keepdims=True)
    v = jnp.var(x, axis=axis, keepdims=True)
    return (x - m) / jnp.sqrt(v + eps)
def _scatter_add(tgt, idx, src, axis=0):
    return tgt.at[idx].add(src)
def _segment_sum(src, seg, n):
    return jax.ops.segment_sum(src, seg, n)

kernel_name = 'mk_conv_seq_d1_conv_nchw256_db4037'

def setup_inputs(seed: int = 0):
    np.random.seed(seed)
    _w = jnp.asarray
    def _rec_inputs():
        import jax
        import jax.numpy as jnp
        _gk = jax.random.key(seed)
        x = -7.109e-05 + 0.9999 * jax.random.normal(jax.random.fold_in(_gk, 1), (16, 256, 128, 128), jnp.float32)
        return x
    x = _rec_inputs()
    def _L0_conv_setup():
        import jax, jax.numpy as jnp
        import numpy as np
        EPS = 1e-12
        NUM_CLASSES = 80

        def _l2_normalize(x, axis):
            n = jnp.sqrt(jnp.sum(x * x, axis=axis, keepdims=True))
            return x / jnp.maximum(n, EPS)
        key = jax.random.key(seed)
        k1, k2, k3, k4 = jax.random.split(key, 4)
        B, C, H, W = (16, 256, 128, 128)
        N = NUM_CLASSES
        features = jax.random.normal(k1, (B, C, H, W), dtype=jnp.float32)
        centroids = jax.random.normal(k2, (N, C), dtype=jnp.float32)
        fc_w = jax.random.normal(k3, (C, C, 1, 1), dtype=jnp.float32) * 0.02
        fc_b = jax.random.normal(k4, (C,), dtype=jnp.float32) * 0.01
        return {'features': features, 'centroids': centroids, 'fc_w': fc_w, 'fc_b': fc_b}
    _L0_conv_all = _L0_conv_setup()
    _L0_conv_in = {k: v for k, v in _L0_conv_all.items() if k in ('centroids', 'fc_w', 'fc_b', )}
    del _L0_conv_all

    return {
        "x": x,
        "L0_conv_centroids": _L0_conv_in["centroids"],
        "L0_conv_fc_w": _L0_conv_in["fc_w"],
        "L0_conv_fc_b": _L0_conv_in["fc_b"],
    }

def reference(x, L0_conv_centroids, L0_conv_fc_w, L0_conv_fc_b):
    import jax
    import jax.numpy as jnp
    def _L0_conv_ref(features, centroids, fc_w, fc_b):
        import jax, jax.numpy as jnp
        import numpy as np
        EPS = 1e-12
        NUM_CLASSES = 80

        def _l2_normalize(x, axis):
            n = jnp.sqrt(jnp.sum(x * x, axis=axis, keepdims=True))
            return x / jnp.maximum(n, EPS)
        N = centroids.shape[0]
        sim = jnp.einsum('bchw,nc->bnhw', _l2_normalize(features, axis=1), _l2_normalize(centroids, axis=1))
        idx = jnp.argmax(sim, axis=1)
        mask = jax.nn.one_hot(idx, N, axis=1, dtype=features.dtype)
        sum_x = jnp.einsum('bnhw,bchw->bnc', mask, features)
        count = jnp.sum(mask, axis=(2, 3))[:, :, None]
        cent = sum_x / jnp.maximum(count, 1.0)
        delta = jnp.einsum('bnhw,bnc->bchw', mask, cent) - features
        alpha = jnp.exp(-jnp.mean(jnp.square(delta), axis=1, keepdims=True))
        x = features + alpha * delta
        out = jnp.einsum('bchw,oc->bohw', x, fc_w[:, :, 0, 0]) + fc_b[None, :, None, None]
        return jax.nn.relu(out)

    def _gn(v, G=32, eps=1e-5):
        B_, C_, H_, W_ = v.shape
        g = v.reshape(B_, G, C_ // G, H_, W_)
        m = jnp.mean(g, axis=(2, 3, 4), keepdims=True)
        s = jnp.var(g, axis=(2, 3, 4), keepdims=True)
        return ((g - m) / jnp.sqrt(s + eps)).reshape(v.shape)

    def _ln_c(v, eps=1e-6):
        m = jnp.mean(v, axis=1, keepdims=True)
        s = jnp.var(v, axis=1, keepdims=True)
        return (v - m) / jnp.sqrt(s + eps)

    def _ln_t(v, eps=1e-5):
        m = jnp.mean(v, axis=-1, keepdims=True)
        s = jnp.var(v, axis=-1, keepdims=True)
        return (v - m) / jnp.sqrt(s + eps)

    def _to_tokens(v):
        B_, C_, H_, W_ = v.shape
        return v.reshape(B_, C_, H_ * W_).transpose(0, 2, 1)
    def _from_tokens(t, like):
        B_, C_, H_, W_ = like.shape
        return t.transpose(0, 2, 1).reshape(B_, C_, H_, W_)

    x = _L0_conv_ref(x, L0_conv_centroids, L0_conv_fc_w, L0_conv_fc_b)
    return x


_drawn_inputs = setup_inputs


def setup_inputs(seed=0):
    import zlib

    import numpy as np

    out = dict(_drawn_inputs(seed))
    spreads = {}
    factors = {}
    for name, (base, spread) in spreads.items():
        noise = np.random.default_rng([zlib.crc32(name.encode()), seed]).standard_normal(out[name].shape)
        drawn = base * np.exp(spread * noise) if base else spread * noise
        out[name] = jnp.asarray(drawn.astype(out[name].dtype))
    for name, factor in factors.items():
        out[name] = (out[name] * factor).astype(out[name].dtype)
    return out
```

```python
from contextlib import ExitStack

import concourse.bass as bass
from concourse import mybir

FP32 = mybir.dt.float32
FP32R = mybir.dt.float32r
BF16 = mybir.dt.bfloat16
I32 = mybir.dt.int32
ALU = mybir.AluOpType
ACT = mybir.ActivationFunctionType
AX_X = mybir.AxisListType.X
EPS = 1e-12


def centre_smoothing_conv_kernel(nc, x, centroids, fc_w, fc_b, out):
    B, C, H, W = x.shape
    N = centroids.shape[0]
    O = fc_w.shape[0]
    P = 128
    KC = C // P
    OC = O // P
    PIX = 512
    T = PIX // P
    BLOCKS = H * W // PIX
    U = 4
    GROUPS = BLOCKS // U
    CX = C + 2

    x_v = x.rearrange("b (k p) h w -> b p k (h w)", p=P)
    out_v = out.rearrange("b (k p) h w -> b p k (h w)", p=P)

    ctx = ExitStack()
    with ctx:
        def sb(name, shape, dt=FP32):
            return ctx.enter_context(nc.sbuf_tensor(name, shape, dt))

        def pb(name, shape, dt=FP32):
            return ctx.enter_context(nc.psum_tensor(name, shape, dt))

        def sem(name):
            return ctx.enter_context(nc.semaphore(name))

        image = sb("image", [P, BLOCKS, KC, PIX])
        stage = sb("stage", [P, U, KC, PIX])
        masks = sb("masks", [P, BLOCKS, T, N], BF16)
        x_hi = sb("x_hi", [P, T, CX], FP32R)
        x_lo = sb("x_lo", [P, T, C], FP32R)
        mask = sb("mask", [P, T, N], FP32R)
        tied = sb("tied", [P, T, N], BF16)
        rank = sb("rank", [P, T, N], BF16)
        order = sb("order", [P, T, N], BF16)
        order_i = sb("order_i", [P, T, N], I32)
        best = sb("best", [P, T])
        best_rank = sb("best_rank", [P, T])
        mask_t = sb("mask_t", [N, PIX], FP32R)
        delta = sb("delta", [P, KC, PIX])
        square = sb("square", [P, KC, PIX])
        sq_sum = sb("sq_sum", [P, PIX])
        alpha = sb("alpha", [P, PIX])
        result = sb("result", [P, 2, OC, PIX])
        centre = sb("centre", [N, C])
        centre_hi = sb("centre_hi", [N, C], FP32R)
        centre_lo = sb("centre_lo", [N, C], FP32R)
        count = sb("count", [N, 2])
        class_t = sb("class_t", [P, KC, N])
        w_t = sb("w_t", [P, KC, O])
        bias = sb("bias", [P, OC])
        zeros = sb("zeros", [P, CX], FP32R)
        ones = sb("ones", [P, P])
        ident = sb("ident", [P, P])
        ident16 = sb("ident16", [P, P], BF16)
        cent_in = centre[:, :]
        cent_sq = sq_sum[0:N, 0:C]
        norm = sb("norm", [N, 6])
        w_in = delta[:, :, 0:C]

        sim_ps = pb("sim_ps", [P, T, N])
        xt_ps = [pb(f"xt_ps{n}", [P, T // 2, C]) for n in range(2)]
        sum_ps = pb("sum_ps", [N, CX])
        centre_ps = [pb(f"centre_ps{n}", [P, PIX]) for n in range(KC)]
        dist_ps = centre_ps[0]
        conv_ps = [pb(f"conv_ps{n}", [P, PIX]) for n in range(OC)]
        mt_ps = conv_ps[1][:, 0:PIX // 2].bitcast(BF16)

        s_const = sem("s_const")
        s_in = sem("s_in")
        s_setup_act = sem("s_setup_act")
        s_setup_dve = sem("s_setup_dve")
        s_setup_pe = sem("s_setup_pe")
        s_load = [sem(f"s_load{n}") for n in range(U)]
        s_copy = [sem(f"s_copy{n}") for n in range(U)]
        s_store = [sem(f"s_store{n}") for n in range(2)]
        s_sim = sem("s_sim")
        s_xt = sem("s_xt")
        s_best = sem("s_best")
        s_mask = sem("s_mask")
        s_mask16 = sem("s_mask16")
        s_hi = sem("s_hi")
        s_lo = sem("s_lo")
        s_sum = sem("s_sum")
        s_cchain = sem("s_cchain")
        s_centre = sem("s_centre")
        s_mt = sem("s_mt")
        s_mtc = sem("s_mtc")
        s_cpix = sem("s_cpix")
        s_delta = sem("s_delta")
        s_square = sem("s_square")
        s_sqsum = sem("s_sqsum")
        s_dist = sem("s_dist")
        s_alpha = sem("s_alpha")
        s_scaled = sem("s_scaled")
        s_moved = sem("s_moved")
        s_conv = sem("s_conv")
        s_result = sem("s_result")

        block = ctx.enter_context(nc.Block())

        def rounds(eng, group, finish, begin=lambda b1: None):
            begin(0)
            with eng.Fori(0, GROUPS) as j:
                group(0, None, j, False)
            finish(0, None)
            with eng.Fori(1, B) as b:
                begin(b)
                group(b, b - 1, 0, True)
                with eng.Fori(1, GROUPS) as j:
                    group(b, b - 1, j, False)
                finish(b, b - 1)
            group(None, B - 1, 0, True)
            with eng.Fori(1, GROUPS) as j:
                group(None, B - 1, j, False)
            finish(None, B - 1)

        def start(eng, *counters):
            for counter in counters:
                eng.sem_inc(counter, 1)

        def done(n):
            return n + 1

        def landed(n):
            return (n + 1) * 16

        def nth(b, j, u):
            return b * BLOCKS + j * U + u

        def place(j, u):
            return bass.ds(j * U + u, 1)

        @block.sync
        def _(sp):
            for counter in (*s_load, *s_copy, *s_store):
                sp.sem_inc(counter, 16)
            sp.dma_start(cent_in, centroids).then_inc(s_in, 16)
            sp.dma_start(w_in, fc_w.rearrange("(k p) c h w -> p k (c h w)", p=P)).then_inc(s_in, 16)
            sp.dma_start(bias[:, :], fc_b.rearrange("(k p) -> p k", p=P),
                         allow_slow_non_contiguous=True).then_inc(s_in, 16)
            with sp.Fori(0, B) as b:
                with sp.Fori(0, GROUPS) as j:
                    for u in range(U):
                        sp.wait_ge(s_copy[u], landed(b * GROUPS + j))
                        sp.dma_start(stage[:, u], x_v[b, :, :, bass.ds((j * U + u) * PIX, PIX)]
                                     ).then_inc(s_load[u], 16)

        @block.gpsimd
        def _(pool):
            start(pool, s_sqsum)
            nc.gpsimd.memset(ident[:, :], 0.0).then_inc(s_const, 1)
            pool.wait_ge(s_const, 1)
            nc.gpsimd.affine_select(out=ident[:, :], in_=ident[:, :], compare_op=ALU.not_equal, fill=1.0, base=0,
                                    pattern=[[-1, P]], channel_multiplier=1).then_inc(s_const, 1)
            nc.gpsimd.iota(order_i[:, :, :], pattern=[[0, T], [-1, N]], base=N,
                           channel_multiplier=0).then_inc(s_const, 1)
            pool.wait_ge(s_const, 3)
            nc.gpsimd.tensor_copy(ident16[:, :], ident[:, :]).then_inc(s_const, 1)
            nc.gpsimd.tensor_copy(order[:, :, :], order_i[:, :, :]).then_inc(s_const, 1)
            nc.gpsimd.memset(ones[:, :], 1.0).then_inc(s_const, 1)
            nc.gpsimd.memset(zeros[:, :].bitcast(FP32), 0.0).then_inc(s_const, 1)
            nc.gpsimd.memset(x_hi[:, :, C:CX].bitcast(FP32), 1.0).then_inc(s_const, 1)

            def group(b1, b2, j, first):
                for u in range(U):
                    if b2 is not None:
                        pool.wait_ge(s_square, done((nth(b2, j, u) + 1) * KC))
                        nc.gpsimd.tensor_tensor(sq_sum[:, :], square[:, 0], square[:, 1],
                                                ALU.add).then_inc(s_sqsum, 1)

            rounds(pool, group, lambda b1, b2: None)

        @block.scalar
        def _(act):
            start(act, s_hi, s_mtc, s_square, s_alpha, s_result)
            act.wait_ge(s_in, 48)
            nc.scalar.activation(cent_sq, cent_in, ACT.Square, accum_out=norm[:, 0:1]).then_inc(s_setup_act, 1)
            act.wait_ge(s_setup_act, 1)
            nc.scalar.activation(norm[:, 1:2], norm[:, 0:1], ACT.Sqrt).then_inc(s_setup_act, 1)
            for k in range(KC):
                act.wait_ge(s_setup_pe, k + 1)
                nc.scalar.activation(w_t[:, k, :], conv_ps[k][:, 0:O], ACT.Copy).then_inc(s_setup_act, 1)

            def convolved(b2, k, slot, i):
                n = nth(b2, *k)
                act.wait_ge(s_store[slot], landed(b2 * (BLOCKS // 2) + k[0] * (U // 2) + k[1] // 2))
                for m, o in enumerate(reversed(range(OC))):
                    act.wait_ge(s_conv, done(n * OC + m + 1))
                    nc.scalar.activation(result[:, slot, o], conv_ps[o][:, :], ACT.Relu,
                                         bias=bias[:, o:o + 1]).then_inc(s_result, 1)
                act.wait_ge(s_result, done((n + 1) * OC))
                act.dma_start(out_v[b2, :, :, bass.ds(i * PIX, PIX)], result[:, slot]).then_inc(s_store[slot], 16)

            def keep(j, u):
                act.dma_start(image[:, place(j, u)].rearrange("p a k n -> p (a k n)"),
                              stage[:, u].rearrange("p k n -> p (k n)")).then_inc(s_copy[u % U], 16)

            def group(b1, b2, j, first):
                for u in range(U):
                    if b2 is not None:
                        h = nth(b2, j, u)
                        act.wait_ge(s_mt, done(h + 1))
                        nc.scalar.activation(mask_t[:, :], mt_ps[0:N, :], ACT.Copy).then_inc(s_mtc, 1)
                    if b1 is not None:
                        g = nth(b1, j, u)
                        for n in range(2):
                            act.wait_ge(s_xt, done(2 * g + n + 1))
                            nc.scalar.activation(x_hi[:, 2 * n:2 * n + 2, 0:C], xt_ps[n][:, :, :],
                                                 ACT.Copy).then_inc(s_hi, 1)
                        if b2 is None:
                            keep(j, u)
                    if b2 is not None:
                        for k in range(KC):
                            act.wait_ge(s_delta, done(h * KC + k + 1))
                            nc.scalar.activation(square[:, k], delta[:, k], ACT.Square).then_inc(s_square, 1)
                        if not (first and u == 0):
                            convolved(b2, (j, u - 1), (u - 1) % 2, j * U + u - 1)
                            if b1 is not None:
                                keep(j, u - 1) if u else keep(j - 1, U - 1)
                        act.wait_ge(s_dist, done(h + 1))
                        nc.scalar.activation(alpha[:, :], dist_ps[:, :], ACT.Exp, scale=-1.0 / C).then_inc(s_alpha, 1)

            def finish(b1, b2):
                if b2 is not None:
                    convolved(b2, (GROUPS - 1, U - 1), (U - 1) % 2, BLOCKS - 1)
                    if b1 is not None:
                        keep(GROUPS - 1, U - 1)

            rounds(act, group, finish)
            for slot in range(2):
                act.wait_ge(s_store[slot], landed(B * BLOCKS // 2))

        @block.vector
        def _(dve):
            start(dve, s_best, s_mask, s_mask16, s_lo, s_cchain, s_centre, s_delta, s_scaled, s_moved)
            squared, root, r, s = (norm[:, n:n + 1] for n in range(4))
            steps = [0]

            def then(ins):
                steps[0] += 1
                ins.then_inc(s_setup_dve, 1)
                dve.wait_ge(s_setup_dve, steps[0])

            dve.wait_ge(s_setup_act, 2)
            then(nc.vector.tensor_scalar(root, root, EPS, None, ALU.max))
            then(nc.vector.reciprocal(r, root))
            then(nc.vector.tensor_tensor(s, squared, r, ALU.mult))
            then(nc.vector.tensor_tensor(s, s, root, ALU.add))
            then(nc.vector.tensor_scalar(s, s, 0.5, EPS, ALU.mult, ALU.max))
            then(nc.vector.reciprocal(r, s))
            then(nc.vector.tensor_scalar(cent_sq, cent_in, r, None, ALU.mult))
            dve.wait_ge(s_setup_pe, KC + 1)
            then(nc.vector.tensor_copy(class_t[:, :, :], sim_ps[:, 0:KC, :]))
            dve.wait_ge(s_const, 8)

            def group(b1, b2, j, first):
                for u in range(U):
                    if b2 is not None:
                        h = nth(b2, j, u)
                        dve.wait_ge(s_copy[u], landed(b2 * GROUPS + j + 1))
                        dve.wait_ge(s_moved, done(h * KC))
                        for k in range(KC):
                            dve.wait_ge(s_cpix, done(h * KC + k + 1))
                            nc.vector.tensor_tensor(delta[:, k], centre_ps[k][:, :],
                                                    image[:, place(j, u), k].rearrange("p a n -> p (a n)"),
                                                    ALU.subtract).then_inc(s_delta, 1)
                    if b1 is not None:
                        g = nth(b1, j, u)
                        dve.wait_ge(s_sim, done(g + 1))
                        nc.vector.reduce_max(best[:, :], sim_ps[:, :, :], AX_X).then_inc(s_best, 1)
                        dve.wait_ge(s_best, done(4 * g + 1))
                        nc.vector.tensor_tensor(tied[:, :, :], sim_ps[:, :, :],
                                                best[:, :].unsqueeze(2).to_broadcast([P, T, N]),
                                                ALU.is_equal).then_inc(s_best, 1)
                        dve.wait_ge(s_best, done(4 * g + 2))
                        nc.vector.tensor_tensor(rank[:, :, :], tied[:, :, :], order[:, :, :],
                                                ALU.mult).then_inc(s_best, 1)
                        dve.wait_ge(s_best, done(4 * g + 3))
                        nc.vector.reduce_max(best_rank[:, :], rank[:, :, :], AX_X).then_inc(s_best, 1)
                        dve.wait_ge(s_best, done(4 * g + 4))
                        nc.vector.tensor_tensor(mask[:, :, :], rank[:, :, :],
                                                best_rank[:, :].unsqueeze(2).to_broadcast([P, T, N]),
                                                ALU.is_equal).then_inc(s_mask, 1)
                        dve.wait_ge(s_mask, done(g + 1))
                        nc.vector.tensor_scalar(masks[:, place(j, u)].rearrange("p a t n -> p (a t n)"),
                                                mask[:, :, :].rearrange("p t n -> p (t n)").bitcast(FP32),
                                                1.0, None, ALU.mult).then_inc(s_mask16, 1)
                        for n in range(2):
                            dve.wait_ge(s_hi, done(2 * g + n + 1))
                            nc.vector.tensor_tensor(x_lo[:, 2 * n:2 * n + 2, :], xt_ps[n][:, :, :],
                                                    x_hi[:, 2 * n:2 * n + 2, 0:C].bitcast(FP32),
                                                    ALU.subtract).then_inc(s_lo, 1)
                    if b2 is not None:
                        dve.wait_ge(s_alpha, done(h + 1))
                        for k in range(KC):
                            nc.vector.tensor_tensor(delta[:, k], delta[:, k], alpha[:, :],
                                                    ALU.mult).then_inc(s_scaled, 1)
                        for k in range(KC):
                            dve.wait_ge(s_scaled, done(h * KC + k + 1))
                            at = image[:, place(j, u), k].rearrange("p a n -> p (a n)")
                            nc.vector.tensor_tensor(at, at, delta[:, k], ALU.add).then_inc(s_moved, 1)

            def finish(b1, b2):
                if b1 is None:
                    return
                dve.wait_ge(s_sum, done((b1 + 1) * BLOCKS))
                nc.vector.tensor_scalar(count[:, 0:1], sum_ps[:, C:C + 1], 1.0, None, ALU.max).then_inc(s_cchain, 1)
                dve.wait_ge(s_cchain, done(b1 * 4 + 1))
                nc.vector.reciprocal(count[:, 1:2], count[:, 0:1]).then_inc(s_cchain, 1)
                dve.wait_ge(s_cchain, done(b1 * 4 + 2))
                nc.vector.tensor_scalar(centre[:, :], sum_ps[:, 0:C], count[:, 1:2], None,
                                        ALU.mult).then_inc(s_cchain, 1)
                dve.wait_ge(s_cchain, done(b1 * 4 + 3))
                nc.vector.tensor_copy(centre_hi[:, :], centre[:, :]).then_inc(s_cchain, 1)
                dve.wait_ge(s_cchain, done(b1 * 4 + 4))
                nc.vector.tensor_tensor(centre_lo[:, :], centre[:, :], centre_hi[:, :].bitcast(FP32),
                                        ALU.subtract).then_inc(s_centre, 1)

            rounds(dve, group, finish)

        @block.tensor
        def _(pe):
            start(pe, s_sim, s_xt, s_sum, s_mt, s_cpix, s_dist, s_conv)
            pe.wait_ge(s_in, 48)
            pe.wait_ge(s_const, 8)
            for k in range(KC):
                for o in range(OC):
                    last = nc.tensor.transpose(conv_ps[k][:, o * P:(o + 1) * P], w_in[:, o, k * P:(k + 1) * P],
                                               ident[:, :])
                last.then_inc(s_setup_pe, 1)
            pe.wait_ge(s_setup_dve, 7)
            for k in range(KC):
                last = nc.tensor.transpose(sim_ps[:, k, :], cent_sq[:, k * P:(k + 1) * P], ident[0:N, 0:N])
            last.then_inc(s_setup_pe, 1)
            pe.wait_ge(s_setup_act, 4)
            pe.wait_ge(s_setup_dve, 8)

            def convolve(n, at):
                pe.wait_ge(s_moved, done((n + 1) * KC))
                pe.wait_ge(s_result, done(n * OC))
                for o in reversed(range(OC)):
                    for k in range(KC):
                        last = nc.tensor.matmul(conv_ps[o][:, :], w_t[:, k, o * P:(o + 1) * P],
                                                image[:, at, k].rearrange("p a n -> p (a n)"),
                                                start=(k == 0), stop=(k == KC - 1))
                    last.then_inc(s_conv, 1)

            def group(b1, b2, j, first):
                for u in range(U):
                    if b2 is not None:
                        h = nth(b2, j, u)
                        pe.wait_ge(s_result, done((h if first and u == 0 else h - 1) * OC))
                        pe.wait_ge(s_mask16, done(h + 1))
                        for t in range(T):
                            last = nc.tensor.transpose(mt_ps[0:N, t * P:(t + 1) * P],
                                                       masks[:, place(j, u), t].rearrange("p a n -> p (a n)"),
                                                       ident16[:, :])
                        last.then_inc(s_mt, 1)
                    if b1 is not None:
                        g = nth(b1, j, u)
                        pe.wait_ge(s_load[u], landed(b1 * GROUPS + j + 1))
                        pe.wait_ge(s_mask, done(g))
                        for t in range(T):
                            for k in range(KC):
                                last = nc.tensor.matmul(sim_ps[:, t, :], stage[:, u, k, t * P:(t + 1) * P],
                                                        class_t[:, k, :], start=(k == 0), stop=(k == KC - 1))
                        last.then_inc(s_sim, 1)
                        pe.wait_ge(s_lo, done(2 * g))
                        for t in range(T):
                            for k in range(KC):
                                last = nc.tensor.transpose(xt_ps[t // 2][:, t % 2, k * P:(k + 1) * P],
                                                           stage[:, u, k, t * P:(t + 1) * P], ident[:, :])
                            if t % 2:
                                last.then_inc(s_xt, 1)
                    if b2 is not None:
                        if first and u == 0:
                            pe.wait_ge(s_centre, done(b2 + 1))
                        pe.wait_ge(s_mtc, done(h + 1))
                        pe.wait_ge(s_alpha, done(h))
                        for k in range(KC):
                            nc.tensor.matmul(centre_ps[k][:, :], centre_hi[:, k * P:(k + 1) * P], mask_t[:, :],
                                             start=True, stop=False)
                            nc.tensor.matmul(centre_ps[k][:, :], centre_lo[:, k * P:(k + 1) * P], mask_t[:, :],
                                             start=False, stop=True).then_inc(s_cpix, 1)
                        if not (first and u == 0):
                            convolve(h - 1, place(j, u - 1))
                        pe.wait_ge(s_sqsum, done(h + 1))
                        nc.tensor.matmul(dist_ps[:, :], ones[:, :], sq_sum[:, :], start=True,
                                         stop=True).then_inc(s_dist, 1)
                    if b1 is not None:
                        pe.wait_ge(s_mask, done(g + 1))
                        for t in range(T):
                            pe.wait_ge(s_lo, done(2 * g + t // 2 + 1))
                            nc.tensor.matmul(sum_ps[:, :], mask[:, t, :], x_hi[:, t, :], start=False, stop=False,
                                             skip_group_check=True)
                            last = nc.tensor.matmul(sum_ps[:, 0:C], mask[:, t, :], x_lo[:, t, :], start=False,
                                                    stop=False, skip_group_check=True)
                        last.then_inc(s_sum, 1)

            def finish(b1, b2):
                if b2 is not None:
                    convolve(nth(b2, GROUPS - 1, U - 1), place(GROUPS - 1, U - 1))

            def begin(b1):
                pe.wait_ge(s_centre, done(b1))
                nc.tensor.matmul(sum_ps[:, :], zeros[:, 0:N], zeros[:, :], start=True, stop=False,
                                 skip_group_check=True)

            rounds(pe, group, finish, begin)


_INS = ["x", "L0_conv_centroids", "L0_conv_fc_w", "L0_conv_fc_b"]


def kernel(**inputs):
    import numpy as _np
    import concourse.bacc as _bacc
    from concourse import mybir as _mybir
    from concourse.bass_utils import run_bass_kernel_spmd as _run

    nc = _bacc.Bacc("TRN2", target_bir_lowering=False, num_devices=1)
    arrays, args = {}, []
    for name in _INS:
        a = _np.ascontiguousarray(inputs[name])
        arrays[f"in_{name}_dram"] = a
        args.append(nc.dram_tensor(f"in_{name}_dram", a.shape, _mybir.dt.from_np(a.dtype), kind="ExternalInput").ap())
    shape = inputs["x"].shape
    out_shape = (shape[0], inputs["L0_conv_fc_w"].shape[0], shape[2], shape[3])
    args.append(nc.dram_tensor("out_0_dram", out_shape, _mybir.dt.float32, kind="ExternalOutput").ap())
    centre_smoothing_conv_kernel(nc, *args)
    r = _run(nc, [arrays], core_ids=[0])
    return r.results[0]["out_0_dram"]
```

```python
from contextlib import ExitStack

import concourse.bass as bass
from concourse import mybir

FP32 = mybir.dt.float32
FP32R = mybir.dt.float32r
BF16 = mybir.dt.bfloat16
I32 = mybir.dt.int32
ALU = mybir.AluOpType
ACT = mybir.ActivationFunctionType
AX_X = mybir.AxisListType.X
EPS = 1e-12


def centre_smoothing_conv_kernel(nc, x, centroids, fc_w, fc_b, out):
    B, C, H, W = x.shape
    N = centroids.shape[0]
    O = fc_w.shape[0]
    P = 128
    KC = C // P
    OC = O // P
    PIX = 512
    T = PIX // P
    BLOCKS = H * W // PIX
    U = 4
    GROUPS = BLOCKS // U
    CX = C + 2

    x_v = x.rearrange("b (k p) h w -> b p k (h w)", p=P)
    out_v = out.rearrange("b (k p) h w -> b p k (h w)", p=P)

    ctx = ExitStack()
    with ctx:
        def sb(name, shape, dt=FP32):
            return ctx.enter_context(nc.sbuf_tensor(name, shape, dt))

        def pb(name, shape, dt=FP32):
            return ctx.enter_context(nc.psum_tensor(name, shape, dt))

        def sem(name):
            return ctx.enter_context(nc.semaphore(name))

        image = sb("image", [P, BLOCKS, KC, PIX])
        stage = sb("stage", [P, U, KC, PIX])
        ranks = sb("ranks", [P, BLOCKS, T])
        x_hi = sb("x_hi", [P, 2, T, CX], FP32R)
        x_lo = sb("x_lo", [P, 2, T, C], FP32R)
        mask = sb("mask", [P, 2, T, N], FP32R)
        mask16 = sb("mask16", [P, T, N], BF16)
        tied = sb("tied", [P, T, N], BF16)
        rank = tied
        order = sb("order", [P, T, N], BF16)
        best = sb("best", [P, T])
        best_rank = sb("best_rank", [P, T])
        mask_t = sb("mask_t", [N, PIX], FP32R)
        delta = sb("delta", [P, KC, PIX])
        square = sb("square", [P, KC, PIX])
        sq_sum = square[:, 0]
        alpha = square[:, 1]
        moved = sb("moved", [P, KC, PIX])
        moved_hi = sb("moved_hi", [P, KC, PIX], FP32R)
        moved_lo = sb("moved_lo", [P, KC, PIX], FP32R)
        result = sb("result", [P, 2, OC, PIX])
        centre = square[0:N, 0, 0:C]
        centre_hi = sb("centre_hi", [N, C], FP32R)
        centre_lo = sb("centre_lo", [N, C], FP32R)
        count = sb("count", [N, 2])
        class_t = sb("class_t", [P, KC, N])
        w_hi = sb("w_hi", [P, KC, O], FP32R)
        w_lo = sb("w_lo", [P, KC, O], FP32R)
        bias = sb("bias", [P, OC])
        zeros = sb("zeros", [P, CX], BF16)
        ones = sb("ones", [P, P])
        ident = sb("ident", [P, P])
        ident16 = sb("ident16", [P, P], BF16)
        norm = sb("norm", [N, 6])
        cent_in = moved[0:N, 1, 0:C]
        cent_sq = square[0:N, 0, 0:C]
        w_in = delta[:, :, 0:C]
        order_i = moved[:, 0, 0:T * N].bitcast(I32)

        sim_ps = pb("sim_ps", [P, T, N])
        xt_ps = [pb(f"xt_ps{n}", [P, T // 2, C]) for n in range(2)]
        sum_ps = pb("sum_ps", [N, CX])
        centre_ps = [pb(f"centre_ps{n}", [P, PIX]) for n in range(KC)]
        dist_ps = centre_ps[0]
        conv_ps = [pb(f"conv_ps{n}", [P, PIX]) for n in range(OC)]
        mt_ps = conv_ps[1][:, 0:PIX // 2].bitcast(BF16)

        s_const = sem("s_const")
        s_in = sem("s_in")
        s_setup_act = sem("s_setup_act")
        s_setup_dve = sem("s_setup_dve")
        s_setup_pe = sem("s_setup_pe")
        s_load = [sem(f"s_load{n}") for n in range(U)]
        s_copy = [sem(f"s_copy{n}") for n in range(U)]
        s_store = [sem(f"s_store{n}") for n in range(2)]
        s_sim = sem("s_sim")
        s_xt = sem("s_xt")
        s_best = sem("s_best")
        s_kept = sem("s_kept")
        s_mask = sem("s_mask")
        s_mask16 = sem("s_mask16")
        s_hi = sem("s_hi")
        s_lo = sem("s_lo")
        s_sum = sem("s_sum")
        s_cchain = sem("s_cchain")
        s_centre = sem("s_centre")
        s_mt = sem("s_mt")
        s_mtc = sem("s_mtc")
        s_cpix = sem("s_cpix")
        s_delta = sem("s_delta")
        s_square = sem("s_square")
        s_sqsum = sem("s_sqsum")
        s_dist = sem("s_dist")
        s_alpha = sem("s_alpha")
        s_scaled = sem("s_scaled")
        s_scaled1 = sem("s_scaled1")
        s_moved = sem("s_moved")
        s_moved_hi = sem("s_moved_hi")
        s_moved_lo = sem("s_moved_lo")
        s_conv = sem("s_conv")
        s_result = sem("s_result")

        block = ctx.enter_context(nc.Block())

        def rounds(eng, group, finish):
            def rest_of_round(b1, b2):
                with eng.Fori(1, GROUPS) as j:
                    group(b1, b2, j, False, False)
                finish(b1, b2)

            group(0, None, 0, True, False)
            rest_of_round(0, None)
            group(1, 0, 0, True, False)
            rest_of_round(1, 0)
            with eng.Fori(2, B) as b:
                group(b, b - 1, 0, True, True)
                rest_of_round(b, b - 1)
            group(None, B - 1, 0, True, True)
            rest_of_round(None, B - 1)

        def start(eng, *counters):
            for counter in counters:
                eng.sem_inc(counter, 1)

        def done(n):
            return n + 1

        def landed(n):
            return (n + 1) * 16

        def nth(b, j, u):
            return b * BLOCKS + j * U + u

        def place(j, u):
            return bass.ds(j * U + u, 1)

        @block.sync
        def _(sp):
            for counter in (*s_load, *s_copy, *s_store):
                sp.sem_inc(counter, 16)
            sp.dma_start(cent_in, centroids).then_inc(s_in, 16)
            sp.dma_start(w_in, fc_w.rearrange("(k p) c h w -> p k (c h w)", p=P)).then_inc(s_in, 16)
            sp.dma_start(bias[:, :], fc_b.rearrange("(k p) -> p k", p=P),
                         allow_slow_non_contiguous=True).then_inc(s_in, 16)
            with sp.Fori(0, B) as b:
                with sp.Fori(0, GROUPS) as j:
                    for u in range(U):
                        sp.wait_ge(s_copy[u], landed(b * GROUPS + j))
                        sp.dma_start(stage[:, u], x_v[b, :, :, bass.ds((j * U + u) * PIX, PIX)]
                                     ).then_inc(s_load[u], 16)

        @block.gpsimd
        def _(pool):
            start(pool, s_scaled1, s_moved_lo)
            nc.gpsimd.memset(ident[:, :], 0.0).then_inc(s_const, 1)
            pool.wait_ge(s_const, 1)
            nc.gpsimd.affine_select(out=ident[:, :], in_=ident[:, :], compare_op=ALU.not_equal, fill=1.0, base=0,
                                    pattern=[[-1, P]], channel_multiplier=1).then_inc(s_const, 1)
            nc.gpsimd.iota(order_i, pattern=[[0, T], [-1, N]], base=N,
                           channel_multiplier=0).then_inc(s_const, 1)
            pool.wait_ge(s_const, 3)
            nc.gpsimd.tensor_copy(ident16[:, :], ident[:, :]).then_inc(s_const, 1)
            nc.gpsimd.tensor_copy(order[:, :, :].rearrange("p t n -> p (t n)"), order_i).then_inc(s_const, 1)
            nc.gpsimd.memset(ones[:, :], 1.0).then_inc(s_const, 1)
            nc.gpsimd.memset(zeros[:, :], 0.0).then_inc(s_const, 1)
            nc.gpsimd.memset(x_hi[:, :, :, C:CX].bitcast(FP32), 1.0).then_inc(s_const, 1)

            def move(n):
                pool.wait_ge(s_alpha, done(n + 1))
                nc.gpsimd.tensor_tensor(delta[:, 1], delta[:, 1], alpha, ALU.mult).then_inc(s_scaled1, 1)
                for k in range(KC):
                    pool.wait_ge(s_moved_hi, done(n * KC + k + 1))
                    nc.gpsimd.tensor_tensor(moved_lo[:, k], moved[:, k], moved_hi[:, k].bitcast(FP32),
                                            ALU.subtract).then_inc(s_moved_lo, 1)

            def group(b1, b2, j, first, carried):
                for u in range(U):
                    if b2 is not None and not (first and u == 0):
                        move(nth(b2, j, u) - 1)

            def finish(b1, b2):
                if b2 is not None:
                    move(nth(b2, GROUPS, -1))

            rounds(pool, group, finish)

        @block.scalar
        def _(act):
            start(act, s_hi, s_mtc, s_square, s_alpha, s_moved_hi, s_result)
            act.wait_ge(s_in, 48)
            nc.scalar.activation(cent_sq, cent_in, ACT.Square, accum_out=norm[:, 0:1]).then_inc(s_setup_act, 1)
            act.wait_ge(s_setup_act, 1)
            nc.scalar.activation(norm[:, 1:2], norm[:, 0:1], ACT.Sqrt).then_inc(s_setup_act, 1)
            nc.scalar.activation(norm[:, 4:5], norm[:, 0:1], ACT.Exp, scale=-1.0)
            for k in range(KC):
                act.wait_ge(s_setup_pe, k + 1)
                nc.scalar.activation(w_hi[:, k, :], conv_ps[k][:, 0:O], ACT.Copy).then_inc(s_setup_act, 1)

            def weigh(n):
                act.wait_ge(s_dist, done(n + 1))
                nc.scalar.activation(alpha, dist_ps[:, :], ACT.Exp, scale=-1.0 / C).then_inc(s_alpha, 1)

            def upper(n):
                for k in range(KC):
                    act.wait_ge(s_moved, done(n * KC + k + 1))
                    nc.scalar.activation(moved_hi[:, k], moved[:, k], ACT.Copy).then_inc(s_moved_hi, 1)

            def upper_x(g, u, n):
                act.wait_ge(s_xt, done(2 * g + n + 1))
                nc.scalar.activation(x_hi[:, u % 2, 2 * n:2 * n + 2, 0:C], xt_ps[n][:, :, :], ACT.Copy).then_inc(s_hi, 1)

            def convolved(b2, j, u):
                n = nth(b2, j, u)
                slot = u % 2
                act.wait_ge(s_store[slot], landed(b2 * (BLOCKS // 2) + j * (U // 2) + u // 2))
                for m, o in enumerate(reversed(range(OC))):
                    act.wait_ge(s_conv, done(n * OC + m + 1))
                    nc.scalar.activation(result[:, slot, o], conv_ps[o][:, :], ACT.Relu,
                                         bias=bias[:, o:o + 1]).then_inc(s_result, 1)
                act.wait_ge(s_result, done((n + 1) * OC))
                act.dma_start(out_v[b2, :, :, bass.ds((j * U + u) * PIX, PIX)], result[:, slot]
                              ).then_inc(s_store[slot], 16)

            def keep(j, u):
                act.dma_start(image[:, place(j, u)].rearrange("p a k n -> p (a k n)"),
                              stage[:, u % U].rearrange("p k n -> p (k n)")).then_inc(s_copy[u % U], 16)

            def group(b1, b2, j, first, carried):
                for u in range(U):
                    behind = not (first and u == 0)
                    if b1 is not None:
                        g = nth(b1, j, u)
                    if b2 is None:
                        upper_x(g, u, 0)
                        upper_x(g, u, 1)
                        keep(j, u)
                        continue
                    h = nth(b2, j, u)
                    if behind:
                        weigh(h - 1)
                    act.wait_ge(s_mt, done(h + 1))
                    nc.scalar.activation(mask_t[:, :], mt_ps[0:N, :], ACT.Copy).then_inc(s_mtc, 1)
                    if behind:
                        upper(h - 1)
                    if b1 is not None:
                        upper_x(g, u, 0)
                        upper_x(g, u, 1)
                        if behind:
                            keep(j, u - 1)
                    for k in range(KC):
                        act.wait_ge(s_delta, done(h * KC + k + 1))
                        nc.scalar.activation(square[:, k], delta[:, k], ACT.Square).then_inc(s_square, 1)
                    if behind:
                        convolved(b2, j, u - 1)
                    elif carried:
                        convolved(b2 - 1, GROUPS, -1)

            def finish(b1, b2):
                if b2 is not None:
                    weigh(nth(b2, GROUPS, -1))
                    upper(nth(b2, GROUPS, -1))
                    if b1 is not None:
                        keep(GROUPS, -1)

            rounds(act, group, finish)
            convolved(B - 1, GROUPS, -1)
            for slot in range(2):
                act.wait_ge(s_store[slot], landed(B * BLOCKS // 2))

        @block.vector
        def _(dve):
            start(dve, s_sqsum, s_best, s_kept, s_mask, s_mask16, s_lo, s_cchain, s_centre, s_delta, s_scaled, s_moved)
            squared, root, r, s = (norm[:, n:n + 1] for n in range(4))
            steps = [0]

            def then(ins):
                steps[0] += 1
                ins.then_inc(s_setup_dve, 1)
                dve.wait_ge(s_setup_dve, steps[0])

            dve.wait_ge(s_setup_act, 2)
            then(nc.vector.tensor_scalar(root, root, EPS, None, ALU.max))
            then(nc.vector.reciprocal(r, root))
            then(nc.vector.tensor_tensor(s, squared, r, ALU.mult))
            then(nc.vector.tensor_tensor(s, s, root, ALU.add))
            then(nc.vector.tensor_scalar(s, s, 0.5, EPS, ALU.mult, ALU.max))
            then(nc.vector.reciprocal(r, s))
            then(nc.vector.tensor_scalar(cent_sq, cent_in, r, None, ALU.mult))
            dve.wait_ge(s_setup_pe, KC + 1)
            then(nc.vector.tensor_copy(class_t[:, :, :], sim_ps[:, 0:KC, :]))
            for k in range(KC):
                dve.wait_ge(s_setup_act, 3 + k)
                then(nc.vector.tensor_tensor(w_lo[:, k, :], conv_ps[k][:, 0:O], w_hi[:, k, :].bitcast(FP32),
                                             ALU.subtract))
            dve.wait_ge(s_const, 8)

            def per_class(v):
                return v.unsqueeze(2).to_broadcast([P, T, N])

            def move(n, j, u):
                dve.wait_ge(s_alpha, done(n + 1))
                nc.vector.tensor_tensor(delta[:, 0], delta[:, 0], alpha, ALU.mult).then_inc(s_scaled, 1)
                for k, scaled in enumerate((s_scaled, s_scaled1)):
                    dve.wait_ge(scaled, done(n + 1))
                    nc.vector.tensor_tensor(moved[:, k], image[:, place(j, u), k].rearrange("p a n -> p (a n)"),
                                            delta[:, k], ALU.add).then_inc(s_moved, 1)

            def rest_x(g, u, n):
                dve.wait_ge(s_hi, done(2 * g + n + 1))
                nc.vector.tensor_tensor(x_lo[:, u % 2, 2 * n:2 * n + 2, :], xt_ps[n][:, :, :],
                                        x_hi[:, u % 2, 2 * n:2 * n + 2, 0:C].bitcast(FP32),
                                        ALU.subtract).then_inc(s_lo, 1)

            def class_mask(n, at):
                dve.wait_ge(s_kept, done(n + 1))
                nc.vector.tensor_tensor(mask16[:, :, :], order[:, :, :],
                                        per_class(ranks[:, at].rearrange("p a t -> p (a t)")),
                                        ALU.is_equal).then_inc(s_mask16, 1)

            def group(b1, b2, j, first, carried):
                for u in range(U):
                    if b2 is not None:
                        h = nth(b2, j, u)
                        if not (first and u == 0):
                            class_mask(h, place(j, u))
                        if not (first and u == 0):
                            move(h - 1, j, u - 1)
                    if b1 is not None:
                        g = nth(b1, j, u)
                        dve.wait_ge(s_sim, done(g + 1))
                        nc.vector.reduce_max(best[:, :], sim_ps[:, :, :], AX_X).then_inc(s_best, 1)
                    if b2 is not None:
                        dve.wait_ge(s_copy[u], landed(b2 * GROUPS + j + 1))
                        dve.wait_ge(s_moved, done(h * KC))
                        for k in range(KC):
                            dve.wait_ge(s_cpix, done(h * KC + k + 1))
                            nc.vector.tensor_tensor(delta[:, k], centre_ps[k][:, :],
                                                    image[:, place(j, u), k].rearrange("p a n -> p (a n)"),
                                                    ALU.subtract).then_inc(s_delta, 1)
                    if b1 is not None:
                        dve.wait_ge(s_best, done(4 * g + 1))
                        nc.vector.tensor_tensor(tied[:, :, :], sim_ps[:, :, :], per_class(best[:, :]),
                                                ALU.is_equal).then_inc(s_best, 1)
                        rest_x(g, u, 0)
                    if b2 is not None:
                        dve.wait_ge(s_square, done((h + 1) * KC))
                        nc.vector.tensor_tensor(sq_sum, square[:, 0], square[:, 1], ALU.add).then_inc(s_sqsum, 1)
                    if b1 is not None:
                        dve.wait_ge(s_best, done(4 * g + 2))
                        nc.vector.tensor_tensor(rank[:, :, :], tied[:, :, :], order[:, :, :],
                                                ALU.mult).then_inc(s_best, 1)
                        rest_x(g, u, 1)
                        dve.wait_ge(s_best, done(4 * g + 3))
                        dve.wait_ge(s_kept, done(g))
                        nc.vector.reduce_max(best_rank[:, :], rank[:, :, :], AX_X).then_inc(s_best, 1)
                        dve.wait_ge(s_best, done(4 * g + 4))
                        nc.vector.tensor_tensor(mask[:, u % 2], order[:, :, :], per_class(best_rank[:, :]),
                                                ALU.is_equal).then_inc(s_mask, 1)
                        if b2 is not None:
                            dve.wait_ge(s_mask16, done(h + 1))
                        nc.vector.tensor_scalar(ranks[:, place(j, u)].rearrange("p a t -> p (a t)"),
                                                best_rank[:, :], 1.0, None, ALU.mult).then_inc(s_kept, 1)

            def finish(b1, b2):
                if b1 is not None:
                    class_mask(nth(b1, 0, 0), place(0, 0))
                if b2 is not None:
                    move(nth(b2, GROUPS, -1), GROUPS, -1)
                if b1 is None:
                    return
                dve.wait_ge(s_sum, done((b1 + 1) * BLOCKS))
                nc.vector.tensor_scalar(count[:, 0:1], sum_ps[:, C:C + 1], 1.0, None, ALU.max).then_inc(s_cchain, 1)
                dve.wait_ge(s_cchain, done(b1 * 4 + 1))
                nc.vector.reciprocal(count[:, 1:2], count[:, 0:1]).then_inc(s_cchain, 1)
                dve.wait_ge(s_cchain, done(b1 * 4 + 2))
                nc.vector.tensor_scalar(centre, sum_ps[:, 0:C], count[:, 1:2], None,
                                        ALU.mult).then_inc(s_cchain, 1)
                dve.wait_ge(s_cchain, done(b1 * 4 + 3))
                nc.vector.tensor_copy(centre_hi[:, :], centre).then_inc(s_cchain, 1)
                dve.wait_ge(s_cchain, done(b1 * 4 + 4))
                nc.vector.tensor_tensor(centre_lo[:, :], centre, centre_hi[:, :].bitcast(FP32),
                                        ALU.subtract).then_inc(s_centre, 1)

            rounds(dve, group, finish)

        @block.tensor
        def _(pe):
            start(pe, s_sim, s_xt, s_sum, s_mt, s_cpix, s_dist, s_conv)
            pe.wait_ge(s_in, 48)
            pe.wait_ge(s_const, 8)
            for k in range(KC):
                for o in range(OC):
                    last = nc.tensor.transpose(conv_ps[k][:, o * P:(o + 1) * P], w_in[:, o, k * P:(k + 1) * P],
                                               ident[:, :])
                last.then_inc(s_setup_pe, 1)
            pe.wait_ge(s_setup_dve, 7)
            for k in range(KC):
                last = nc.tensor.transpose(sim_ps[:, k, :], cent_sq[:, k * P:(k + 1) * P], ident[0:N, 0:N])
            last.then_inc(s_setup_pe, 1)
            pe.wait_ge(s_setup_act, 4)
            pe.wait_ge(s_setup_dve, 10)

            def convolve(n):
                pe.wait_ge(s_result, done(n * OC))
                for k in range(KC):
                    pe.wait_ge(s_moved_hi, done(n * KC + k + 1))
                    for o in reversed(range(OC)):
                        for w in (w_hi, w_lo):
                            nc.tensor.matmul(conv_ps[o][:, :], w[:, k, o * P:(o + 1) * P], moved_hi[:, k],
                                             start=(k == 0 and w is w_hi), stop=False)
                for k in range(KC):
                    pe.wait_ge(s_moved_lo, done(n * KC + k + 1))
                    for o in reversed(range(OC)):
                        last = nc.tensor.matmul(conv_ps[o][:, :], w_hi[:, k, o * P:(o + 1) * P], moved_lo[:, k],
                                                start=False, stop=(k == KC - 1))
                        if k == KC - 1:
                            last.then_inc(s_conv, 1)

            def distance(n):
                pe.wait_ge(s_sqsum, done(n + 1))
                nc.tensor.matmul(dist_ps[:, :], ones[:, :], sq_sum, start=True, stop=True).then_inc(s_dist, 1)

            def pick_centres(h, b2, wait_centre):
                if wait_centre:
                    pe.wait_ge(s_centre, done(b2 + 1))
                pe.wait_ge(s_mtc, done(h + 1))
                pe.wait_ge(s_alpha, done(h))
                for k in range(KC):
                    nc.tensor.matmul(centre_ps[k][:, :], centre_hi[:, k * P:(k + 1) * P], mask_t[:, :],
                                     start=True, stop=False)
                    nc.tensor.matmul(centre_ps[k][:, :], centre_lo[:, k * P:(k + 1) * P], mask_t[:, :],
                                     start=False, stop=True).then_inc(s_cpix, 1)

            def clear_sums(b1):
                pe.wait_ge(s_centre, done(b1))
                nc.tensor.matmul(sum_ps[:, :], zeros[:, 0:N], zeros[:, :], start=True, stop=False,
                                 skip_group_check=True)

            def add_to_sums(n, u):
                pe.wait_ge(s_mask, done(n + 1))
                pe.wait_ge(s_lo, done(2 * (n + 1)))
                for t in range(T):
                    nc.tensor.matmul(sum_ps[:, :], mask[:, u % 2, t, :], x_hi[:, u % 2, t, :], start=False,
                                     stop=False, skip_group_check=True)
                    last = nc.tensor.matmul(sum_ps[:, 0:C], mask[:, u % 2, t, :], x_lo[:, u % 2, t, :],
                                            start=False, stop=False, skip_group_check=True)
                last.then_inc(s_sum, 1)

            def group(b1, b2, j, first, carried):
                for u in range(U):
                    behind = not (first and u == 0)
                    convolve_behind = behind or carried

                    def products(tiles):
                        for t in tiles:
                            for k in range(KC):
                                last = nc.tensor.matmul(sim_ps[:, t, :], stage[:, u, k, t * P:(t + 1) * P],
                                                        class_t[:, k, :], start=(k == 0), stop=(k == KC - 1))
                        return last

                    if b1 is not None:
                        g = nth(b1, j, u)
                        pe.wait_ge(s_load[u], landed(b1 * GROUPS + j + 1))
                        if behind:
                            pe.wait_ge(s_best, done(4 * g - 2))
                        else:
                            pe.wait_ge(s_mask, done(g))
                        products(range(T // 2))
                    if b2 is not None and behind:
                        distance(nth(b2, j, u) - 1)
                    if b1 is not None:
                        products(range(T // 2, T)).then_inc(s_sim, 1)
                    if b2 is not None:
                        h = nth(b2, j, u)
                        pe.wait_ge(s_result, done((h - 1 if convolve_behind else h) * OC))
                        pe.wait_ge(s_mask16, done(h + 1))
                        for t in range(T):
                            last = nc.tensor.transpose(mt_ps[0:N, t * P:(t + 1) * P], mask16[:, t, :],
                                                       ident16[:, :])
                        last.then_inc(s_mt, 1)
                    if b1 is not None:
                        pe.wait_ge(s_lo, done(2 * g))
                        for t in range(T):
                            for k in range(KC):
                                last = nc.tensor.transpose(xt_ps[t // 2][:, t % 2, k * P:(k + 1) * P],
                                                           stage[:, u, k, t * P:(t + 1) * P], ident[:, :])
                            if t % 2:
                                last.then_inc(s_xt, 1)
                    if b2 is not None:
                        pick_centres(h, b2, not behind)
                    if b1 is not None and behind:
                        if first and u == 1:
                            clear_sums(b1)
                        add_to_sums(g - 1, u - 1)
                    if b2 is not None and convolve_behind:
                        convolve(h - 1)

            def finish(b1, b2):
                if b2 is not None:
                    distance(nth(b2, GROUPS, -1))
                if b1 is not None:
                    add_to_sums(nth(b1, GROUPS, -1), -1)

            rounds(pe, group, finish)
            convolve(B * BLOCKS - 1)


_INS = ["x", "L0_conv_centroids", "L0_conv_fc_w", "L0_conv_fc_b"]


def kernel(**inputs):
    import numpy as _np
    import concourse.bacc as _bacc
    from concourse import mybir as _mybir
    from concourse.bass_utils import run_bass_kernel_spmd as _run

    nc = _bacc.Bacc("TRN2", target_bir_lowering=False, num_devices=1)
    arrays, args = {}, []
    for name in _INS:
        a = _np.ascontiguousarray(inputs[name])
        arrays[f"in_{name}_dram"] = a
        args.append(nc.dram_tensor(f"in_{name}_dram", a.shape, _mybir.dt.from_np(a.dtype), kind="ExternalInput").ap())
    shape = inputs["x"].shape
    out_shape = (shape[0], inputs["L0_conv_fc_w"].shape[0], shape[2], shape[3])
    args.append(nc.dram_tensor("out_0_dram", out_shape, _mybir.dt.float32, kind="ExternalOutput").ap())
    centre_smoothing_conv_kernel(nc, *args)
    r = _run(nc, [arrays], core_ids=[0])
    return r.results[0]["out_0_dram"]
```

```python
from contextlib import ExitStack

import concourse.bass as bass
from concourse import mybir

FP32 = mybir.dt.float32
FP32R = mybir.dt.float32r
BF16 = mybir.dt.bfloat16
I32 = mybir.dt.int32
ALU = mybir.AluOpType
ACT = mybir.ActivationFunctionType
AX_X = mybir.AxisListType.X
EPS = 1e-12


def centre_smoothing_conv_kernel(nc, x, centroids, fc_w, fc_b, out):
    B, C, H, W = x.shape
    N = centroids.shape[0]
    O = fc_w.shape[0]
    P = 128
    KC = C // P
    OC = O // P
    PIX = 512
    T = PIX // P
    BLOCKS = H * W // PIX
    U = 4
    GROUPS = BLOCKS // U
    CX = C + 2

    x_v = x.rearrange("b (k p) h w -> b p k (h w)", p=P)
    out_v = out.rearrange("b (k p) h w -> b p k (h w)", p=P)

    ctx = ExitStack()
    with ctx:
        def sb(name, shape, dt=FP32):
            return ctx.enter_context(nc.sbuf_tensor(name, shape, dt))

        def pb(name, shape, dt=FP32):
            return ctx.enter_context(nc.psum_tensor(name, shape, dt))

        def sem(name):
            return ctx.enter_context(nc.semaphore(name))

        def bank(ps):
            return ps[:, :] if len(ps.shape) == 2 else ps[:, :, :].rearrange("p t n -> p (t n)")

        image = sb("image", [P, BLOCKS, KC, PIX])
        stage = sb("stage", [P, U, KC, PIX])
        ranks = sb("ranks", [P, BLOCKS + 1, T])
        x_hi = sb("x_hi", [P, 2, T, CX], FP32R)
        x_lo = sb("x_lo", [P, T, C], FP32R)
        mask = sb("mask", [P, 2, T, N], FP32R)
        mask16 = sb("mask16", [P, T, N], BF16)
        tied = sb("tied", [P, T, N], BF16)
        rank = tied
        order = sb("order", [P, T, N], BF16)
        best = sb("best", [P, T])
        best_rank = sb("best_rank", [P, T])
        mask_t = sb("mask_t", [N, PIX], FP32R)
        delta = sb("delta", [P, 2, KC, PIX])
        square = sb("square", [P, KC, PIX])
        sq_sum = square[:, 0]
        alpha = sb("alpha", [P, PIX])
        sq_hi = sb("sq_hi", [P, PIX], FP32R)
        sq_lo = sb("sq_lo", [P, PIX], FP32R)
        moved_hi = sb("moved_hi", [P, KC, PIX], FP32R)
        moved_lo = sb("moved_lo", [P, KC, PIX], FP32R)
        result = sb("result", [P, 2, OC, PIX])
        centre = square[0:N, 0, 0:C]
        centre_hi = sb("centre_hi", [N, C], FP32R)
        centre_lo = sb("centre_lo", [N, C], FP32R)
        count = sb("count", [N, 2])
        class_t = sb("class_t", [P, KC, N])
        w_hi = sb("w_hi", [P, KC, O], FP32R)
        w_lo = sb("w_lo", [P, KC, O], FP32R)
        bias = sb("bias", [P, OC])
        zeros = sb("zeros", [P, CX], BF16)
        ones_r = sb("ones_r", [P, P], FP32R)
        ones = ones_r[:, :].bitcast(FP32)
        ident = sb("ident", [P, P])
        ident16 = sb("ident16", [P, P], BF16)
        norm = sb("norm", [N, 6])
        cent_in = delta[0:N, 1, 1, 0:C]
        cent_sq = square[0:N, 0, 0:C]
        w_in = delta[:, 0, :, 0:C]
        order_i = delta[:, 1, 0, 0:T * N].bitcast(I32)

        sim_ps = pb("sim_ps", [P, T, N])
        xt_ps = [pb(f"xt_ps{n}", [P, T // 2, C]) for n in range(2)]
        sum_bank = pb("sum_bank", [P, PIX])
        sum_ps = sum_bank[0:N, 0:CX]
        centre_ps = [pb(f"centre_ps{n}", [P, PIX]) for n in range(KC)]
        dist_ps = bank(xt_ps[1])
        conv_ps = [pb(f"conv_ps{n}", [P, PIX]) for n in range(OC)]
        mt_ps = conv_ps[1][:, 0:PIX // 2].bitcast(BF16)

        delta_last = [stage[:, n] for n in range(2)]
        square_last = [stage[:, 2 + n] for n in range(2)]
        centre_last = [centre_ps, xt_ps]
        dist_last = sum_bank[:, :]
        mt_last = sim_ps[:, :, :].rearrange("p t n -> p (t n)")[:, 0:PIX // 2].bitcast(BF16)

        s_const = sem("s_const")
        s_in = sem("s_in")
        s_setup_act = sem("s_setup_act")
        s_setup_dve = sem("s_setup_dve")
        s_setup_pe = sem("s_setup_pe")
        s_load = [sem(f"s_load{n}") for n in range(U)]
        s_copy = [sem(f"s_copy{n}") for n in range(U)]
        s_store = [sem(f"s_store{n}") for n in range(2)]
        s_sim = sem("s_sim")
        s_xt = sem("s_xt")
        s_best = sem("s_best")
        s_kept = sem("s_kept")
        s_mask = sem("s_mask")
        s_mask16 = sem("s_mask16")
        s_hi = sem("s_hi")
        s_lo = sem("s_lo")
        s_sum = sem("s_sum")
        s_cchain = sem("s_cchain")
        s_centre = sem("s_centre")
        s_mt = sem("s_mt")
        s_mtc = sem("s_mtc")
        s_cpix = sem("s_cpix")
        s_delta = sem("s_delta")
        s_square = sem("s_square")
        s_sqsum = sem("s_sqsum")
        s_sq_hi = sem("s_sq_hi")
        s_sq_lo = sem("s_sq_lo")
        s_dist = sem("s_dist")
        s_alpha = sem("s_alpha")
        s_scaled = sem("s_scaled")
        s_scaled1 = sem("s_scaled1")
        s_moved = sem("s_moved")
        s_moved_hi = sem("s_moved_hi")
        s_moved_lo = sem("s_moved_lo")
        s_conv = sem("s_conv")
        s_result = sem("s_result")

        block = ctx.enter_context(nc.Block())

        def rounds(eng, group, finish):
            def rest_of_round(b1, b2):
                with eng.Fori(1, GROUPS) as j:
                    group(b1, b2, j, False, False)
                finish(b1, b2)

            group(0, None, 0, True, False)
            rest_of_round(0, None)
            group(1, 0, 0, True, False)
            rest_of_round(1, 0)
            with eng.Fori(2, B) as b:
                group(b, b - 1, 0, True, True)
                rest_of_round(b, b - 1)

        def last_round(eng, step):
            def group(j, steps):
                for u in range(steps):
                    step(j, u)

            group(0, U)
            with eng.Fori(1, GROUPS - 1) as j:
                group(j, U)
            group(GROUPS - 1, U)
            group(GROUPS, 2)

        def there(j, u):
            return not isinstance(j, int) or 0 <= j * U + u < BLOCKS

        LAST = (B - 1) * BLOCKS

        def start(eng, *counters):
            for counter in counters:
                eng.sem_inc(counter, 1)

        def done(n):
            return n + 1

        def landed(n):
            return (n + 1) * 16

        def nth(b, j, u):
            return b * BLOCKS + j * U + u

        def place(j, u):
            return bass.ds(j * U + u, 1)

        @block.sync
        def _(sp):
            for counter in (*s_load, *s_copy, *s_store):
                sp.sem_inc(counter, 16)
            sp.dma_start(cent_in, centroids).then_inc(s_in, 16)
            sp.dma_start(w_in, fc_w.rearrange("(k p) c h w -> p k (c h w)", p=P)).then_inc(s_in, 16)
            sp.dma_start(bias[:, :], fc_b.rearrange("(k p) -> p k", p=P),
                         allow_slow_non_contiguous=True).then_inc(s_in, 16)
            with sp.Fori(0, B) as b:
                with sp.Fori(0, GROUPS) as j:
                    for u in range(U):
                        sp.wait_ge(s_copy[u], landed(b * GROUPS + j))
                        sp.dma_start(stage[:, u], x_v[b, :, :, bass.ds((j * U + u) * PIX, PIX)]
                                     ).then_inc(s_load[u], 16)

        @block.gpsimd
        def _(pool):
            start(pool, s_scaled1, s_moved_lo, s_sq_lo)
            nc.gpsimd.memset(ident[:, :], 0.0).then_inc(s_const, 1)
            pool.wait_ge(s_const, 1)
            nc.gpsimd.affine_select(out=ident[:, :], in_=ident[:, :], compare_op=ALU.not_equal, fill=1.0, base=0,
                                    pattern=[[-1, P]], channel_multiplier=1).then_inc(s_const, 1)
            nc.gpsimd.iota(order_i, pattern=[[0, T], [-1, N]], base=N,
                           channel_multiplier=0).then_inc(s_const, 1)
            pool.wait_ge(s_const, 3)
            nc.gpsimd.tensor_copy(ident16[:, :], ident[:, :]).then_inc(s_const, 1)
            nc.gpsimd.tensor_copy(order[:, :, :].rearrange("p t n -> p (t n)"), order_i).then_inc(s_const, 1)
            nc.gpsimd.memset(ones, 1.0).then_inc(s_const, 1)
            nc.gpsimd.memset(zeros[:, :], 0.0).then_inc(s_const, 1)
            nc.gpsimd.memset(x_hi[:, :, :, C:CX].bitcast(FP32), 1.0).then_inc(s_const, 1)

            def move(n, delta, moved, alpha=alpha[:, :]):
                pool.wait_ge(s_alpha, done(n + 1))
                nc.gpsimd.tensor_tensor(delta[:, 1], delta[:, 1], alpha, ALU.mult).then_inc(s_scaled1, 1)
                for k in range(KC):
                    pool.wait_ge(s_moved_hi, done(n * KC + k + 1))
                    nc.gpsimd.tensor_tensor(moved_lo[:, k], moved[:, k], moved_hi[:, k].bitcast(FP32),
                                            ALU.subtract).then_inc(s_moved_lo, 1)

            def group(b1, b2, j, first, carried):
                for u in range(U):
                    if b2 is None:
                        continue
                    h = nth(b2, j, u)
                    if not (first and u == 0):
                        move(h - 1, delta[:, (u - 1) % 2], delta[:, (u - 1) % 2])
                    pool.wait_ge(s_sq_hi, done(h + 1))
                    nc.gpsimd.tensor_tensor(sq_lo[:, :], sq_sum, sq_hi[:, :].bitcast(FP32), ALU.subtract).then_inc(s_sq_lo, 1)

            def finish(b1, b2):
                if b2 is not None:
                    move(nth(b2, GROUPS, -1), delta[:, 1], delta[:, 1])

            rounds(pool, group, finish)

            def step(j, u):
                if there(j, u - 1):
                    move(LAST + j * U + u - 1, delta_last[(u - 1) % 2], delta[:, (u - 1) % 2], square_last[(u - 1) % 2][:, 1])

            last_round(pool, step)

        @block.scalar
        def _(act):
            start(act, s_hi, s_mtc, s_square, s_sq_hi, s_alpha, s_moved_hi, s_result)
            act.wait_ge(s_in, 48)
            nc.scalar.activation(cent_sq, cent_in, ACT.Square, accum_out=norm[:, 0:1]).then_inc(s_setup_act, 1)
            act.wait_ge(s_setup_act, 1)
            nc.scalar.activation(norm[:, 1:2], norm[:, 0:1], ACT.Sqrt).then_inc(s_setup_act, 1)
            nc.scalar.activation(norm[:, 4:5], norm[:, 0:1], ACT.Exp, scale=-1.0)
            for k in range(KC):
                act.wait_ge(s_setup_pe, k + 1)
                nc.scalar.activation(w_hi[:, k, :], conv_ps[k][:, 0:O], ACT.Copy).then_inc(s_setup_act, 1)

            def weigh(n, alpha=alpha[:, :], dist_ps=dist_ps):
                act.wait_ge(s_dist, done(n + 1))
                nc.scalar.activation(alpha, dist_ps, ACT.Exp, scale=-1.0 / C).then_inc(s_alpha, 1)

            def upper(n, u, k):
                act.wait_ge(s_moved, done(n * KC + k + 1))
                nc.scalar.activation(moved_hi[:, k], delta[:, u % 2, k], ACT.Copy).then_inc(s_moved_hi, 1)

            def upper_x(g, u, n):
                act.wait_ge(s_xt, done(2 * g + n + 1))
                nc.scalar.activation(x_hi[:, u % 2, 2 * n:2 * n + 2, 0:C], xt_ps[n][:, :, :], ACT.Copy).then_inc(s_hi, 1)

            def convolved(b2, j, u):
                n = nth(b2, j, u)
                slot = u % 2
                act.wait_ge(s_store[slot], landed(b2 * (BLOCKS // 2) + j * (U // 2) + u // 2))
                for o in range(OC):
                    act.wait_ge(s_conv, done(n * OC + o + 1))
                    nc.scalar.activation(result[:, slot, o], conv_ps[o][:, :], ACT.Relu,
                                         bias=bias[:, o:o + 1]).then_inc(s_result, 1)

            def send(b2, j, u):
                slot = u % 2
                act.wait_ge(s_result, done((nth(b2, j, u) + 1) * OC))
                act.dma_start(out_v[b2, :, :, bass.ds((j * U + u) * PIX, PIX)], result[:, slot]
                              ).then_inc(s_store[slot], 16)

            def squares(n, k, delta, square=square):
                act.wait_ge(s_delta, done(n * KC + k + 1))
                nc.scalar.activation(square[:, k], delta[:, k], ACT.Square).then_inc(s_square, 1)

            def transposed_mask(n, mt_ps=mt_ps):
                act.wait_ge(s_mt, done(n + 1))
                nc.scalar.activation(mask_t[:, :], mt_ps[0:N, :], ACT.Copy).then_inc(s_mtc, 1)

            def keep(j, u):
                act.dma_start(image[:, place(j, u)].rearrange("p a k n -> p (a k n)"),
                              stage[:, u % U].rearrange("p k n -> p (k n)")).then_inc(s_copy[u % U], 16)

            def group(b1, b2, j, first, carried):
                for u in range(U):
                    behind = not (first and u == 0)
                    g = nth(b1, j, u)
                    if b2 is None:
                        upper_x(g, u, 0)
                        upper_x(g, u, 1)
                        keep(j, u)
                        continue
                    h = nth(b2, j, u)
                    queued = (b2, j, u - 2) if not (first and u < 2) else (b2 - 1, GROUPS, -1) if carried else None
                    if behind:
                        weigh(h - 1)
                        if queued:
                            convolved(*queued)
                    squares(h, 0, delta[:, u % 2])
                    if behind:
                        upper(h - 1, u - 1, 0)
                    squares(h, 1, delta[:, u % 2])
                    act.wait_ge(s_cpix, done((h + 1) * KC))
                    transposed_mask(h + 1)
                    if behind:
                        upper(h - 1, u - 1, 1)
                        keep(j, u - 1)
                    upper_x(g, u, 0)
                    act.wait_ge(s_sqsum, done(h + 1))
                    nc.scalar.activation(sq_hi[:, :], sq_sum, ACT.Copy).then_inc(s_sq_hi, 1)
                    upper_x(g, u, 1)
                    if behind and queued:
                        send(*queued)

            def finish(b1, b2):
                if b2 is not None:
                    weigh(nth(b2, GROUPS, -1))
                    convolved(b2, GROUPS, -2)
                    for k in range(KC):
                        upper(nth(b2, GROUPS, -1), -1, k)
                    keep(GROUPS, -1)
                    send(b2, GROUPS, -2)
                else:
                    transposed_mask(0)

            rounds(act, group, finish)

            def step(j, u):
                h = LAST + j * U + u
                if there(j, u + 1):
                    act.wait_ge(s_cpix, done((h + 1) * KC))
                    transposed_mask(h + 1, mt_last)
                if there(j, u):
                    for k in range(KC):
                        squares(h, k, delta_last[u % 2], square_last[u % 2])
                if there(j, u - 2):
                    convolved(B - 1, j, u - 2)
                    send(B - 1, j, u - 2)
                if there(j, u):
                    weigh(h, square_last[u % 2][:, 1], dist_last)
                if there(j, u - 1):
                    for k in range(KC):
                        upper(h - 1, u - 1, k)

            convolved(B - 2, GROUPS, -1)
            send(B - 2, GROUPS, -1)
            for u in range(2, 4):
                act.wait_ge(s_copy[u], landed(B * GROUPS))
            last_round(act, step)
            for slot in range(2):
                act.wait_ge(s_store[slot], landed(B * BLOCKS // 2))

        @block.vector
        def _(dve):
            start(dve, s_sqsum, s_best, s_kept, s_mask, s_mask16, s_lo, s_cchain, s_centre, s_delta, s_scaled, s_moved)
            squared, root, r, s = (norm[:, n:n + 1] for n in range(4))
            steps = [0]

            def then(ins):
                steps[0] += 1
                ins.then_inc(s_setup_dve, 1)
                dve.wait_ge(s_setup_dve, steps[0])

            dve.wait_ge(s_setup_act, 2)
            then(nc.vector.tensor_scalar(root, root, EPS, None, ALU.max))
            then(nc.vector.reciprocal(r, root))
            then(nc.vector.tensor_tensor(s, squared, r, ALU.mult))
            then(nc.vector.tensor_tensor(s, s, root, ALU.add))
            then(nc.vector.tensor_scalar(s, s, 0.5, EPS, ALU.mult, ALU.max))
            then(nc.vector.reciprocal(r, s))
            then(nc.vector.tensor_scalar(cent_sq, cent_in, r, None, ALU.mult))
            dve.wait_ge(s_setup_pe, KC + 1)
            then(nc.vector.tensor_copy(class_t[:, :, :], sim_ps[:, 0:KC, :]))
            for k in range(KC):
                dve.wait_ge(s_setup_act, 3 + k)
                then(nc.vector.tensor_tensor(w_lo[:, k, :], conv_ps[k][:, 0:O], w_hi[:, k, :].bitcast(FP32),
                                             ALU.subtract))
            dve.wait_ge(s_const, 8)

            def per_class(v):
                return v.unsqueeze(2).to_broadcast([P, T, N])

            def scale(n, delta, alpha=alpha[:, :]):
                dve.wait_ge(s_alpha, done(n + 1))
                nc.vector.tensor_tensor(delta[:, 0], delta[:, 0], alpha, ALU.mult).then_inc(s_scaled, 1)

            def move(n, j, u, k, delta):
                dve.wait_ge((s_scaled, s_scaled1)[k], done(n + 1))
                nc.vector.tensor_tensor(moved(u)[:, k], image[:, place(j, u), k].rearrange("p a n -> p (a n)"),
                                        delta[:, k], ALU.add).then_inc(s_moved, 1)

            def moved(u):
                return delta[:, u % 2]

            def rest_x(g, u, n):
                dve.wait_ge(s_hi, done(2 * g + n + 1))
                dve.wait_ge(s_sum, done(g))
                nc.vector.tensor_tensor(x_lo[:, 2 * n:2 * n + 2, :], xt_ps[n][:, :, :],
                                        x_hi[:, u % 2, 2 * n:2 * n + 2, 0:C].bitcast(FP32),
                                        ALU.subtract).then_inc(s_lo, 1)

            def differences(n, j, u, k, delta, centre_ps=centre_ps):
                dve.wait_ge(s_cpix, done(n * KC + k + 1))
                nc.vector.tensor_tensor(delta[:, k], bank(centre_ps[k]),
                                        image[:, place(j, u), k].rearrange("p a n -> p (a n)"),
                                        ALU.subtract).then_inc(s_delta, 1)

            def sum_squares(n, square=square):
                dve.wait_ge(s_square, done((n + 1) * KC))
                nc.vector.tensor_tensor(square[:, 0], square[:, 0], square[:, 1], ALU.add).then_inc(s_sqsum, 1)

            def class_mask(n, at):
                dve.wait_ge(s_kept, done(n + 1))
                nc.vector.tensor_tensor(mask16[:, :, :], order[:, :, :],
                                        per_class(ranks[:, at].rearrange("p a t -> p (a t)")),
                                        ALU.is_equal).then_inc(s_mask16, 1)

            def group(b1, b2, j, first, carried):
                for u in range(U):
                    if b2 is not None:
                        h = nth(b2, j, u)
                        dve.wait_ge(s_mt, done(h + 1))
                        class_mask(h + 1, place(j, u + 1))
                        dve.wait_ge(s_copy[u], landed(b2 * GROUPS + j + 1))
                        if not (first and u == 0) or carried:
                            dve.wait_ge(s_moved_lo, done((h - 1) * KC))
                        differences(h, j, u, 0, moved(u))
                        if not (first and u == 0):
                            scale(h - 1, moved(u - 1))
                            move(h - 1, j, u - 1, 0, moved(u - 1))
                        differences(h, j, u, 1, moved(u))
                        if not (first and u == 0):
                            move(h - 1, j, u - 1, 1, moved(u - 1))
                    g = nth(b1, j, u)
                    dve.wait_ge(s_sim, done(g + 1))
                    nc.vector.reduce_max(best[:, :], sim_ps[:, :, :], AX_X).then_inc(s_best, 1)
                    dve.wait_ge(s_best, done(4 * g + 1))
                    nc.vector.tensor_tensor(tied[:, :, :], sim_ps[:, :, :], per_class(best[:, :]),
                                            ALU.is_equal).then_inc(s_best, 1)
                    if b2 is not None:
                        sum_squares(h)
                    dve.wait_ge(s_best, done(4 * g + 2))
                    nc.vector.tensor_tensor(rank[:, :, :], tied[:, :, :], order[:, :, :],
                                            ALU.mult).then_inc(s_best, 1)
                    rest_x(g, u, 0)
                    dve.wait_ge(s_best, done(4 * g + 3))
                    dve.wait_ge(s_kept, done(g))
                    nc.vector.reduce_max(best_rank[:, :], rank[:, :, :], AX_X).then_inc(s_best, 1)
                    rest_x(g, u, 1)
                    dve.wait_ge(s_best, done(4 * g + 4))
                    nc.vector.tensor_tensor(mask[:, u % 2], order[:, :, :], per_class(best_rank[:, :]),
                                            ALU.is_equal).then_inc(s_mask, 1)
                    if b2 is not None:
                        dve.wait_ge(s_mask16, done(h + 1))
                    kept_at = place(GROUPS, 0) if first and u == 0 else place(j, u)
                    nc.vector.tensor_scalar(ranks[:, kept_at].rearrange("p a t -> p (a t)"),
                                            best_rank[:, :], 1.0, None, ALU.mult).then_inc(s_kept, 1)

            def finish(b1, b2):
                if b2 is None:
                    class_mask(0, place(GROUPS, 0))
                if b2 is not None:
                    scale(nth(b2, GROUPS, -1), moved(-1))
                    for k in range(KC):
                        move(nth(b2, GROUPS, -1), GROUPS, -1, k, moved(-1))
                dve.wait_ge(s_sum, done((b1 + 1) * BLOCKS))
                nc.vector.tensor_scalar(count[:, 0:1], sum_ps[:, C:C + 1], 1.0, None, ALU.max).then_inc(s_cchain, 1)
                dve.wait_ge(s_cchain, done(b1 * 4 + 1))
                nc.vector.reciprocal(count[:, 1:2], count[:, 0:1]).then_inc(s_cchain, 1)
                dve.wait_ge(s_cchain, done(b1 * 4 + 2))
                nc.vector.tensor_scalar(centre, sum_ps[:, 0:C], count[:, 1:2], None,
                                        ALU.mult).then_inc(s_cchain, 1)
                dve.wait_ge(s_cchain, done(b1 * 4 + 3))
                nc.vector.tensor_copy(centre_hi[:, :], centre).then_inc(s_cchain, 1)
                dve.wait_ge(s_cchain, done(b1 * 4 + 4))
                nc.vector.tensor_tensor(centre_lo[:, :], centre, centre_hi[:, :].bitcast(FP32),
                                        ALU.subtract).then_inc(s_centre, 1)

            rounds(dve, group, finish)

            def step(j, u):
                h = LAST + j * U + u
                if there(j, u):
                    dve.wait_ge(s_moved, done((h - 1) * KC))
                    for k in range(KC):
                        differences(h, j, u, k, delta_last[u % 2], centre_last[u % 2])
                if there(j, u - 1):
                    scale(h - 1, delta_last[(u - 1) % 2], square_last[(u - 1) % 2][:, 1])
                if there(j, u):
                    sum_squares(h, square_last[u % 2])
                if there(j, u - 1):
                    dve.wait_ge(s_moved_lo, done((h - 1) * KC))
                    for k in range(KC):
                        move(h - 1, j, u - 1, k, delta_last[(u - 1) % 2])
                if there(j, u + 2):
                    dve.wait_ge(s_mt, done(h + 2))
                    class_mask(h + 2, place(j, u + 2))

            dve.wait_ge(s_mt, done(LAST + 1))
            class_mask(LAST + 1, place(0, 1))
            for u in range(U):
                dve.wait_ge(s_copy[u], landed(B * GROUPS))
            last_round(dve, step)

        @block.tensor
        def _(pe):
            start(pe, s_sim, s_xt, s_sum, s_mt, s_cpix, s_dist, s_conv)
            pe.wait_ge(s_in, 48)
            pe.wait_ge(s_const, 8)
            for k in range(KC):
                for o in range(OC):
                    last = nc.tensor.transpose(conv_ps[k][:, o * P:(o + 1) * P], w_in[:, o, k * P:(k + 1) * P],
                                               ident[:, :])
                last.then_inc(s_setup_pe, 1)
            pe.wait_ge(s_setup_dve, 7)
            for k in range(KC):
                last = nc.tensor.transpose(sim_ps[:, k, :], cent_sq[:, k * P:(k + 1) * P], ident[0:N, 0:N])
            last.then_inc(s_setup_pe, 1)
            pe.wait_ge(s_setup_act, 4)
            pe.wait_ge(s_setup_dve, 10)

            def convolve(n, masks=None):
                pe.wait_ge(s_result, done(n * OC))
                for k in range(KC):
                    pe.wait_ge(s_moved_hi, done(n * KC + k + 1))
                    for o in range(OC):
                        if masks is not None and k == 0 and o == OC - 1:
                            pe.wait_ge(s_mtc, masks)
                        for w in (w_hi, w_lo):
                            nc.tensor.matmul(conv_ps[o][:, :], w[:, k, o * P:(o + 1) * P], moved_hi[:, k],
                                             start=(k == 0 and w is w_hi), stop=False)
                for k in range(KC):
                    pe.wait_ge(s_moved_lo, done(n * KC + k + 1))
                    for o in range(OC):
                        last = nc.tensor.matmul(conv_ps[o][:, :], w_hi[:, k, o * P:(o + 1) * P], moved_lo[:, k],
                                                start=False, stop=(k == KC - 1))
                        if k == KC - 1:
                            last.then_inc(s_conv, 1)

            def distance(n):
                pe.wait_ge(s_sq_lo, done(n + 1))
                nc.tensor.matmul(dist_ps, ones_r[:, :], sq_hi[:, :], start=True, stop=False)
                nc.tensor.matmul(dist_ps, ones_r[:, :], sq_lo[:, :], start=False, stop=True).then_inc(s_dist, 1)

            def distance_last(n, dist_ps, sq_sum):
                pe.wait_ge(s_sqsum, done(n + 1))
                nc.tensor.matmul(dist_ps, ones, sq_sum, start=True, stop=True).then_inc(s_dist, 1)

            def transpose_mask(n, mt_ps=mt_ps):
                pe.wait_ge(s_mask16, done(n + 1))
                for t in range(T):
                    last = nc.tensor.transpose(mt_ps[0:N, t * P:(t + 1) * P], mask16[:, t, :], ident16[:, :])
                last.then_inc(s_mt, 1)

            def pick_centres(n, centre_ps=centre_ps):
                pe.wait_ge(s_mtc, done(n + 1))
                for k in range(KC):
                    nc.tensor.matmul(bank(centre_ps[k]), centre_hi[:, k * P:(k + 1) * P], mask_t[:, :],
                                     start=True, stop=False)
                    nc.tensor.matmul(bank(centre_ps[k]), centre_lo[:, k * P:(k + 1) * P], mask_t[:, :],
                                     start=False, stop=True).then_inc(s_cpix, 1)

            def clear_sums(b1):
                pe.wait_ge(s_centre, done(b1))
                nc.tensor.matmul(sum_ps, zeros[:, 0:N], zeros[:, :], start=True, stop=False,
                                 skip_group_check=True)

            def add_to_sums(n, u):
                pe.wait_ge(s_mask, done(n + 1))
                pe.wait_ge(s_lo, done(2 * (n + 1)))
                for t in range(T):
                    nc.tensor.matmul(sum_ps, mask[:, u % 2, t, :], x_hi[:, u % 2, t, :], start=False,
                                     stop=False, skip_group_check=True)
                    last = nc.tensor.matmul(sum_ps[:, 0:C], mask[:, u % 2, t, :], x_lo[:, t, :],
                                            start=False, stop=False, skip_group_check=True)
                last.then_inc(s_sum, 1)

            def next_mask(h, convolve_behind):
                pe.wait_ge(s_result, done((h - 1 if convolve_behind else h) * OC))
                transpose_mask(h + 1)

            def group(b1, b2, j, first, carried):
                for u in range(U):
                    behind = not (first and u == 0)
                    convolve_behind = behind or carried

                    def products(tiles):
                        for t in tiles:
                            for k in range(KC):
                                last = nc.tensor.matmul(sim_ps[:, t, :], stage[:, u, k, t * P:(t + 1) * P],
                                                        class_t[:, k, :], start=(k == 0), stop=(k == KC - 1))
                        return last

                    if b2 is not None:
                        h = nth(b2, j, u)
                    if b2 is not None and behind:
                        pe.wait_ge(s_delta, done(h * KC))
                        pick_centres(h)
                        pe.wait_ge(s_lo, done(2 * nth(b1, j, u)))
                        distance(h - 1)
                    g = nth(b1, j, u)
                    pe.wait_ge(s_load[u], landed(b1 * GROUPS + j + 1))
                    if behind:
                        pe.wait_ge(s_best, done(4 * g - 2))
                    else:
                        pe.wait_ge(s_mask, done(g))
                    products(range(T)).then_inc(s_sim, 1)
                    pe.wait_ge(s_lo, done(2 * g))
                    if b2 is not None:
                        pe.wait_ge(s_alpha, done(h))
                    for t in range(T):
                        for k in range(KC):
                            last = nc.tensor.transpose(xt_ps[t // 2][:, t % 2, k * P:(k + 1) * P],
                                                       stage[:, u, k, t * P:(t + 1) * P], ident[:, :])
                        if t % 2:
                            last.then_inc(s_xt, 1)
                    if b2 is not None and behind:
                        next_mask(h, convolve_behind)
                    if b2 is not None and not behind:
                        pe.wait_ge(s_centre, done(b2 + 1))
                        pe.wait_ge(s_delta, done(h * KC))
                        pick_centres(h)
                        next_mask(h, convolve_behind)
                    if behind:
                        if first and u == 1:
                            clear_sums(b1)
                        add_to_sums(g - 1, u - 1)
                    if b2 is not None and convolve_behind:
                        convolve(h - 1, masks=done(h + 2))

            def finish(b1, b2):
                if b2 is None:
                    transpose_mask(0)
                else:
                    pe.wait_ge(s_lo, done(2 * (b1 + 1) * BLOCKS))
                    distance(nth(b2, GROUPS, -1))
                add_to_sums(nth(b1, GROUPS, -1), -1)

            rounds(pe, group, finish)

            def step(j, u):
                h = LAST + j * U + u
                if there(j, u - 2):
                    convolve(h - 2)
                if there(j, u + 1):
                    pick_centres(h + 1, centre_last[(u + 1) % 2])
                if there(j, u):
                    pe.wait_ge(s_alpha, done(h))
                    distance_last(h, dist_last, square_last[u % 2][:, 0])
                if there(j, u + 2):
                    transpose_mask(h + 2, mt_last)

            convolve(LAST - 1)
            pe.wait_ge(s_centre, done(B))
            pick_centres(LAST, centre_last[0])
            transpose_mask(LAST + 1, mt_last)
            last_round(pe, step)


_INS = ["x", "L0_conv_centroids", "L0_conv_fc_w", "L0_conv_fc_b"]


def kernel(**inputs):
    import numpy as _np
    import concourse.bacc as _bacc
    from concourse import mybir as _mybir
    from concourse.bass_utils import run_bass_kernel_spmd as _run

    nc = _bacc.Bacc("TRN2", target_bir_lowering=False, num_devices=1)
    arrays, args = {}, []
    for name in _INS:
        a = _np.ascontiguousarray(inputs[name])
        arrays[f"in_{name}_dram"] = a
        args.append(nc.dram_tensor(f"in_{name}_dram", a.shape, _mybir.dt.from_np(a.dtype), kind="ExternalInput").ap())
    shape = inputs["x"].shape
    out_shape = (shape[0], inputs["L0_conv_fc_w"].shape[0], shape[2], shape[3])
    args.append(nc.dram_tensor("out_0_dram", out_shape, _mybir.dt.float32, kind="ExternalOutput").ap())
    centre_smoothing_conv_kernel(nc, *args)
    r = _run(nc, [arrays], core_ids=[0])
    return r.results[0]["out_0_dram"]
```
